# Optimizing a Trainium2 kernel written in Bass

```python
import numpy as np
import jax
import jax.numpy as jnp

def _softmax(x, axis=-1):
    return jax.nn.softmax(x, axis=axis)

def _gelu(x):
    return jax.nn.gelu(x, approximate=True)

def _silu(x):
    return jax.nn.silu(x)

def _sigmoid(x):
    return jax.nn.sigmoid(x)

def _layernorm(x, axis=-1, eps=1e-05):
    m = jnp.mean(x, axis=axis, keepdims=True)
    v = jnp.var(x, axis=axis, keepdims=True)
    return (x - m) / jnp.sqrt(v + eps)

def _scatter_add(tgt, idx, src, axis=0):
    return tgt.at[idx].add(src)

def _segment_sum(src, seg, n):
    return jax.ops.segment_sum(src, seg, n)
kernel_name = 'mk_dlrm_tower_d1_rec_r8_925222'

def setup_inputs(seed: int=0):
    np.random.seed(seed)
    _w = jnp.asarray

    def _rec_inputs():
        import jax
        import jax.numpy as jnp
        _tk = jax.random.key(seed)
        ids = jnp.stack([jax.random.randint(jax.random.fold_in(_tk, 200 + f), (2048,), 0, v, jnp.int32) for f, v in enumerate([1250, 1250, 125000, 12500, 12500, 12500, 1000, 12500, 1250, 12500, 1000, 12500, 1000, 12500, 1000, 1250, 1000, 1000, 1000, 1000, 1250, 1250, 1000, 12500, 1250, 1250])], axis=1)
        tbl_0 = 0.05 * jax.random.normal(jax.random.fold_in(_tk, 500 + 0), (1250, 128), jnp.float32)
        tbl_1 = 0.05 * jax.random.normal(jax.random.fold_in(_tk, 500 + 1), (1250, 128), jnp.float32)
        tbl_2 = 0.05 * jax.random.normal(jax.random.fold_in(_tk, 500 + 2), (125000, 128), jnp.float32)
        tbl_3 = 0.05 * jax.random.normal(jax.random.fold_in(_tk, 500 + 3), (12500, 128), jnp.float32)
        tbl_4 = 0.05 * jax.random.normal(jax.random.fold_in(_tk, 500 + 4), (12500, 128), jnp.float32)
        tbl_5 = 0.05 * jax.random.normal(jax.random.fold_in(_tk, 500 + 5), (12500, 128), jnp.float32)
        tbl_6 = 0.05 * jax.random.normal(jax.random.fold_in(_tk, 500 + 6), (1000, 128), jnp.float32)
        tbl_7 = 0.05 * jax.random.normal(jax.random.fold_in(_tk, 500 + 7), (12500, 128), jnp.float32)
        tbl_8 = 0.05 * jax.random.normal(jax.random.fold_in(_tk, 500 + 8), (1250, 128), jnp.float32)
        tbl_9 = 0.05 * jax.random.normal(jax.random.fold_in(_tk, 500 + 9), (12500, 128), jnp.float32)
        tbl_10 = 0.05 * jax.random.normal(jax.random.fold_in(_tk, 500 + 10), (1000, 128), jnp.float32)
        tbl_11 = 0.05 * jax.random.normal(jax.random.fold_in(_tk, 500 + 11), (12500, 128), jnp.float32)
        tbl_12 = 0.05 * jax.random.normal(jax.random.fold_in(_tk, 500 + 12), (1000, 128), jnp.float32)
        tbl_13 = 0.05 * jax.random.normal(jax.random.fold_in(_tk, 500 + 13), (12500, 128), jnp.float32)
        tbl_14 = 0.05 * jax.random.normal(jax.random.fold_in(_tk, 500 + 14), (1000, 128), jnp.float32)
        tbl_15 = 0.05 * jax.random.normal(jax.random.fold_in(_tk, 500 + 15), (1250, 128), jnp.float32)
        tbl_16 = 0.05 * jax.random.normal(jax.random.fold_in(_tk, 500 + 16), (1000, 128), jnp.float32)
        tbl_17 = 0.05 * jax.random.normal(jax.random.fold_in(_tk, 500 + 17), (1000, 128), jnp.float32)
        tbl_18 = 0.05 * jax.random.normal(jax.random.fold_in(_tk, 500 + 18), (1000, 128), jnp.float32)
        tbl_19 = 0.05 * jax.random.normal(jax.random.fold_in(_tk, 500 + 19), (1000, 128), jnp.float32)
        tbl_20 = 0.05 * jax.random.normal(jax.random.fold_in(_tk, 500 + 20), (1250, 128), jnp.float32)
        tbl_21 = 0.05 * jax.random.normal(jax.random.fold_in(_tk, 500 + 21), (1250, 128), jnp.float32)
        tbl_22 = 0.05 * jax.random.normal(jax.random.fold_in(_tk, 500 + 22), (1000, 128), jnp.float32)
        tbl_23 = 0.05 * jax.random.normal(jax.random.fold_in(_tk, 500 + 23), (12500, 128), jnp.float32)
        tbl_24 = 0.05 * jax.random.normal(jax.random.fold_in(_tk, 500 + 24), (1250, 128), jnp.float32)
        tbl_25 = 0.05 * jax.random.normal(jax.random.fold_in(_tk, 500 + 25), (1250, 128), jnp.float32)
        _rk = jax.random.fold_in(_tk, 7)
        r_bottom_output = -0.000520686 + 1.00062 * jax.random.normal(jax.random.fold_in(_rk, 101), (2048, 128), jnp.float32)
        W_top1 = 0.0456912 * jax.random.normal(jax.random.fold_in(_tk, 801), (479, 512), jnp.float32)
        W_top2 = 0.0441942 * jax.random.normal(jax.random.fold_in(_tk, 802), (512, 256), jnp.float32)
        W_top3 = 0.0625 * jax.random.normal(jax.random.fold_in(_tk, 803), (256, 1), jnp.float32)
        b_top1 = jnp.zeros((512,), jnp.float32)
        b_top2 = jnp.zeros((256,), jnp.float32)
        return (r_bottom_output, ids, tbl_0, tbl_1, tbl_2, tbl_3, tbl_4, tbl_5, tbl_6, tbl_7, tbl_8, tbl_9, tbl_10, tbl_11, tbl_12, tbl_13, tbl_14, tbl_15, tbl_16, tbl_17, tbl_18, tbl_19, tbl_20, tbl_21, tbl_22, tbl_23, tbl_24, tbl_25, W_top1, b_top1, W_top2, b_top2, W_top3)
    r_bottom_output, ids, tbl_0, tbl_1, tbl_2, tbl_3, tbl_4, tbl_5, tbl_6, tbl_7, tbl_8, tbl_9, tbl_10, tbl_11, tbl_12, tbl_13, tbl_14, tbl_15, tbl_16, tbl_17, tbl_18, tbl_19, tbl_20, tbl_21, tbl_22, tbl_23, tbl_24, tbl_25, W_top1, b_top1, W_top2, b_top2, W_top3 = _rec_inputs()

    def _L0_rec_setup():
        import jax, jax.numpy as jnp
        import numpy as np
        NUM_FEATURES = 27
        _TRIU_I, _TRIU_J = np.triu_indices(NUM_FEATURES, k=1)
        key = jax.random.key(seed)
        k1, k2 = jax.random.split(key)
        bottom_output = jax.random.normal(k1, (2048, 128), dtype=jnp.float32)
        embeddings = jax.random.normal(k2, (2048, 26, 128), dtype=jnp.float32)
        return {'bottom_output': bottom_output, 'embeddings': embeddings}
    _L0_rec_all = _L0_rec_setup()
    _L0_rec_in = {k: v for k, v in _L0_rec_all.items() if k in ()}
    del _L0_rec_all
    return {'r_bottom_output': r_bottom_output, 'ids': ids, 'tbl_0': tbl_0, 'tbl_1': tbl_1, 'tbl_2': tbl_2, 'tbl_3': tbl_3, 'tbl_4': tbl_4, 'tbl_5': tbl_5, 'tbl_6': tbl_6, 'tbl_7': tbl_7, 'tbl_8': tbl_8, 'tbl_9': tbl_9, 'tbl_10': tbl_10, 'tbl_11': tbl_11, 'tbl_12': tbl_12, 'tbl_13': tbl_13, 'tbl_14': tbl_14, 'tbl_15': tbl_15, 'tbl_16': tbl_16, 'tbl_17': tbl_17, 'tbl_18': tbl_18, 'tbl_19': tbl_19, 'tbl_20': tbl_20, 'tbl_21': tbl_21, 'tbl_22': tbl_22, 'tbl_23': tbl_23, 'tbl_24': tbl_24, 'tbl_25': tbl_25, 'W_top1': W_top1, 'b_top1': b_top1, 'W_top2': W_top2, 'b_top2': b_top2, 'W_top3': W_top3}

def reference(r_bottom_output, ids, tbl_0, tbl_1, tbl_2, tbl_3, tbl_4, tbl_5, tbl_6, tbl_7, tbl_8, tbl_9, tbl_10, tbl_11, tbl_12, tbl_13, tbl_14, tbl_15, tbl_16, tbl_17, tbl_18, tbl_19, tbl_20, tbl_21, tbl_22, tbl_23, tbl_24, tbl_25, W_top1, b_top1, W_top2, b_top2, W_top3):
    import jax
    import jax.numpy as jnp

    def _L0_rec_ref(bottom_output, embeddings):
        import jax, jax.numpy as jnp
        import numpy as np
        NUM_FEATURES = 27
        _TRIU_I, _TRIU_J = np.triu_indices(NUM_FEATURES, k=1)
        all_emb = jnp.concatenate([bottom_output[:, None, :], embeddings], axis=1)
        gram = jnp.einsum('bfd,bgd->bfg', all_emb, all_emb)
        return gram[:, _TRIU_I, _TRIU_J]
    e = jnp.stack([tbl_0[ids[:, 0]], tbl_1[ids[:, 1]], tbl_2[ids[:, 2]], tbl_3[ids[:, 3]], tbl_4[ids[:, 4]], tbl_5[ids[:, 5]], tbl_6[ids[:, 6]], tbl_7[ids[:, 7]], tbl_8[ids[:, 8]], tbl_9[ids[:, 9]], tbl_10[ids[:, 10]], tbl_11[ids[:, 11]], tbl_12[ids[:, 12]], tbl_13[ids[:, 13]], tbl_14[ids[:, 14]], tbl_15[ids[:, 15]], tbl_16[ids[:, 16]], tbl_17[ids[:, 17]], tbl_18[ids[:, 18]], tbl_19[ids[:, 19]], tbl_20[ids[:, 20]], tbl_21[ids[:, 21]], tbl_22[ids[:, 22]], tbl_23[ids[:, 23]], tbl_24[ids[:, 24]], tbl_25[ids[:, 25]]], axis=1)
    z = _L0_rec_ref(r_bottom_output, e)
    z = z.reshape(z.shape[0], -1)
    h = jnp.concatenate([z, r_bottom_output], axis=1)
    h = jnp.maximum(h @ W_top1 + b_top1, 0.0)
    h = jnp.maximum(h @ W_top2 + b_top2, 0.0)
    y = h @ W_top3
    return y

_drawn_inputs = setup_inputs


def setup_inputs(seed=0):
    import zlib

    import numpy as np

    out = dict(_drawn_inputs(seed))
    spreads = {'b_top1': (0.0, 0.1), 'b_top2': (0.0, 0.1)}
    factors = {}
    for name, (base, spread) in spreads.items():
        noise = np.random.default_rng([zlib.crc32(name.encode()), seed]).standard_normal(out[name].shape)
        drawn = base * np.exp(spread * noise) if base else spread * noise
        out[name] = jnp.asarray(drawn.astype(out[name].dtype))
    for name, factor in factors.items():
        out[name] = (out[name] * factor).astype(out[name].dtype)
    return out
```

```python
from contextlib import ExitStack

import concourse.bass as bass
from concourse import mybir


def pair_row(i, j, features):
    return i * features - i * (i + 1) // 2 + j - i - 1


def dlrm_tower(nc, bottom, ids, tables, w1, b1, w2, b2, w3, y_out):
    f32, f32r, i32 = mybir.dt.float32, mybir.dt.float32r, mybir.dt.int32
    ACT = mybir.ActivationFunctionType
    ALU = mybir.AluOpType

    BATCH, D = bottom.shape
    TABLES = len(tables)
    F = TABLES + 1
    P = 128
    TILE = P
    HALVES = 2
    UNIT = TILE * HALVES
    UNITS = BATCH // UNIT
    SLOTS = 2 * HALVES
    H1, H2 = w1.shape[1], w2.shape[1]
    N1, N2 = H1 // P, H2 // P

    FB = 4
    GROUPS = -(-F // FB)
    FPAD = GROUPS * FB
    J = F - 1
    Q = 4
    QP = P // Q
    XB = 16
    BANK = 512
    CH = -(-J // Q)
    JS = [(r * CH, min(J, (r + 1) * CH)) for r in range(Q)]
    CHUNKS = CH + 1
    PAIRS = F * (F - 1) // 2

    ctx = ExitStack()
    with ctx:
        def sb(name, shape, dt):
            return ctx.enter_context(nc.sbuf_tensor(name, shape, dt))

        def pb(name, shape):
            return ctx.enter_context(nc.psum_tensor(name, shape, f32))

        def sem(name):
            return ctx.enter_context(nc.semaphore(name))

        emb = [sb(f"emb{s}", [P, F, D], f32) for s in range(SLOTS)]
        idx = [sb(f"idx{s}", [P, TABLES], i32) for s in range(SLOTS)]
        xt = sb("xt", [P, UNIT, FPAD], f32)
        pair_hi = sb("pair_hi", [P, CH, UNIT], f32r)
        pair_lo = sb("pair_lo", [P, CH, UNIT], f32r)
        bot_hi = sb("bot_hi", [P, 2, UNIT], f32r)
        bot_lo = sb("bot_lo", [P, 2, UNIT], f32r)
        w1_hi = sb("w1_hi", [P, CHUNKS, H1], f32r)
        w1_lo = sb("w1_lo", [P, CHUNKS, H1], f32r)
        w2_hi = sb("w2_hi", [P, N1, H2], f32r)
        w2_lo = sb("w2_lo", [P, N1, H2], f32r)
        w3_sb = sb("w3_sb", [P, N2], f32)
        b1_sb = sb("b1_sb", [P, N1], f32)
        b2_sb = sb("b2_sb", [P, N2], f32)
        h1_f = sb("h1_f", [P, UNIT], f32)
        h1_hi = sb("h1_hi", [P, N1, UNIT], f32r)
        h1_lo = sb("h1_lo", [P, N1, UNIT], f32r)
        h2_sb = sb("h2_sb", [P, N2, UNIT], f32)
        y_sb = sb("y_sb", [1, UNIT], f32)
        ident = sb("ident", [P, P], f32)

        w1_stage = emb[2][:, :, :].rearrange("p f d -> p (f d)")
        w1_bot_stage = emb[3][:, 0:H1 // D, :].rearrange("p f d -> p (f d)")
        w2_stage = emb[3][:, H1 // D:H1 // D + N1 * H2 // D, :].rearrange("p f d -> p (f d)")
        IN2 = F * D // H1
        w1_rest = emb[3][:, 12:12 + (CH - IN2) * H1 // D, :].rearrange("p f d -> p (f d)")

        turned = pb("turned", [P, 2, FB, P])
        grams = pb("grams", [P, 2 * HALVES, BANK])
        layer = pb("layer", [P, 2, BANK])

        gathered = [[sem(f"gathered{s}_{g}") for g in range(GROUPS)] for s in range(SLOTS)]
        idx_in = [sem(f"idx_in{s}") for s in range(SLOTS)]
        bottom_in = [sem(f"bottom_in{s}") for s in range(SLOTS)]
        stage_zero = sem("stage_zero")
        w1_in = sem("w1_in")
        w2_in = sem("w2_in")
        small_in = sem("small_in")
        w_hi = sem("w_hi")
        w_split = sem("w_split")
        pad_zero = sem("pad_zero")
        ident_zero = sem("ident_zero")
        ident_ready = sem("ident_ready")
        tile_begun = sem("tile_begun")
        turned_ready = sem("turned_ready")
        xt_ready = sem("xt_ready")
        bot_hi_ready = sem("bot_hi_ready")
        bot_lo_ready = sem("bot_lo_ready")
        gram_ready = sem("gram_ready")
        pair_hi_ready = sem("pair_hi_ready")
        pair_lo_ready = sem("pair_lo_ready")
        layer1_done = sem("layer1_done")
        h1_hi_ready = sem("h1_hi_ready")
        h1_f_ready = sem("h1_f_ready")
        h1_lo_ready = sem("h1_lo_ready")
        layer2_done = sem("layer2_done")
        h2_ready = sem("h2_ready")
        layer3_done = sem("layer3_done")
        y_ready = sem("y_ready")
        y_stored = sem("y_stored")

        block = ctx.enter_context(nc.Block())

        def group(g):
            return range(g * FB, min((g + 1) * FB, F))

        def over_units(engine, step):
            step(0, 0)
            with engine.Fori(0, (UNITS - 2) // 2) as v:
                step(v * 2 + 1, 1)
                step(v * 2 + 2, 0)
            step(UNITS - 1, 1)

        def first(u):
            return isinstance(u, int) and u == 0

        def gram_view(h, q, r):
            lo, hi = JS[r]
            bank = grams[QP * q:QP * q + J, 2 * h:2 * h + 2, 0:XB * J]
            return bank.rearrange("p b (x j) -> p j b x", j=J)[:, lo:hi, :, :]

        def pair_view(buffer, h, q, r):
            lo, hi = JS[r]
            at = h * TILE + q * QP
            part = buffer[QP * r:QP * r + J, 0:hi - lo, at:at + QP]
            return part.rearrange("p j (b x) -> p j b x", b=2)

        def w1_piece(i, r):
            lo, hi = JS[r]
            start = max(i, lo)
            row = pair_row(i, start + 1, F)
            out = []
            for c0, c1, stage, base in ((start - lo, min(hi - lo, IN2), w1_stage, 0),
                                        (max(start - lo, IN2), hi - lo, w1_rest, IN2)):
                if c1 > c0:
                    at = row + c0 - (start - lo)
                    dst = stage[QP * r + i:QP * r + i + 1, (c0 - base) * H1:(c1 - base) * H1]
                    out.append((dst, w1[at:at + c1 - c0, :].rearrange("(a c) n -> a (c n)", a=1)))
            return out

        PIECES = [[p for r in rs for i in range(JS[r][1]) for p in w1_piece(i, r)]
                  for rs in ((0, 3), (1, 2))]

        @block.sync
        def _(sp):
            def load_tile(t, s):
                sp.dma_start(idx[s][:, :], ids[bass.ds(t * TILE, TILE), :]).then_inc(idx_in[s], 16)
                sp.dma_start(emb[s][:, 0, :], bottom[bass.ds(t * TILE, TILE), :]).then_inc(bottom_in[s], 16)

            for s in range(HALVES):
                load_tile(s, s)
            sp.wait_ge(stage_zero, 2)
            for dst, src in PIECES[0]:
                sp.dma_start(dst, src).then_inc(w1_in, 16)
            sp.wait_ge(w_split, 1)
            for s in range(HALVES, SLOTS):
                load_tile(s, s)

            def step(u, par):
                for h in range(HALVES):
                    sp.wait_ge(turned_ready, (u - 1) * HALVES * GROUPS + (h + 1) * GROUPS)
                    load_tile((u + 1) * HALVES + h, (1 - par) * HALVES + h)

            def store(u):
                sp.wait_ge(y_ready, u + 1)
                sp.dma_start(y_out[bass.ds(u * UNIT, UNIT), :].rearrange("(a n) c -> a (n c)", a=1),
                             y_sb[:, :]).then_inc(y_stored, 16)

            with sp.Fori(0, (UNITS - 2) // 2) as v:
                step(v * 2 + 1, 1)
                store(v * 2)
                step(v * 2 + 2, 0)
                store(v * 2 + 1)
            store(UNITS - 2)
            store(UNITS - 1)
            sp.wait_ge(y_stored, UNITS * 16)

        @block.gpsimd
        def _(pool):
            pool.memset(ident[:, :], 0.0).then_inc(ident_zero, 1)
            pool.wait_ge(ident_zero, 1)
            pool.affine_select(out=ident[:, :], in_=ident[:, :], compare_op=ALU.not_equal, fill=1.0,
                               base=0, pattern=[[-1, P]], channel_multiplier=1).then_inc(ident_ready, 1)
            with pool.Fori(0, UNITS // 2) as v:
                for s in range(SLOTS):
                    pool.wait_ge(idx_in[s], (v + 1) * 16)
                    pool.sem_inc(tile_begun, 1)
                    for g in range(GROUPS):
                        for f in group(g):
                            if f == 0:
                                continue
                            pool.indirect_dma_start(
                                emb[s][:, f, :], None, tables[f - 1],
                                bass.IndirectOffsetOnAxis(ap=idx[s][:, f - 1:f], axis=0),
                            ).then_inc(gathered[s][g], 16)

        @block.scalar
        def _(act):
            act.dma_start(b1_sb[:, :], b1).then_inc(small_in, 16)
            act.dma_start(b2_sb[:, :], b2).then_inc(small_in, 16)
            act.dma_start(w3_sb[:, :], w3).then_inc(small_in, 16)
            act.dma_start(w1_bot_stage, w1[PAIRS:PAIRS + D, :]).then_inc(w1_in, 16)
            act.dma_start(w2_stage.rearrange("p (k n) -> p k n", k=N1),
                          w2.rearrange("(k p) n -> p k n", p=P)).then_inc(w2_in, 16)
            act.wait_ge(stage_zero, 2)
            for dst, src in PIECES[1]:
                act.dma_start(dst, src).then_inc(w1_in, 16)
            act.wait_ge(small_in, 3 * 16)

            act.wait_ge(w2_in, 16)
            nc.scalar.activation(w2_hi[:, :, :].rearrange("p k n -> p (k n)"), w2_stage,
                                 ACT.Copy).then_inc(w_hi, 1)
            act.wait_ge(w1_in, (len(PIECES[0]) + len(PIECES[1]) + 1) * 16)
            flat = w1_hi[:, :, :].rearrange("p c n -> p (c n)")
            nc.scalar.activation(flat[:, 0:IN2 * H1], w1_stage[:, 0:IN2 * H1], ACT.Copy).then_inc(w_hi, 1)
            nc.scalar.activation(flat[:, IN2 * H1:CH * H1], w1_rest, ACT.Copy).then_inc(w_hi, 1)
            nc.scalar.activation(flat[:, CH * H1:], w1_bot_stage, ACT.Copy).then_inc(w_hi, 1)

            def turned_out(u, par):
                for h in range(HALVES):
                    for g in range(GROUPS):
                        n = (HALVES * h + h * (GROUPS - HALVES) + g)
                        act.wait_ge(turned_ready, u * HALVES * GROUPS + n + 1)
                        fs = group(g)
                        nc.scalar.activation(
                            xt[:, h * TILE:(h + 1) * TILE, fs[0]:fs[-1] + 1],
                            turned[:, n % 2, 0:len(fs), :].rearrange("p f b -> p b f"),
                            ACT.Copy).then_inc(xt_ready, 1)
                act.wait_ge(xt_ready, (u + 1) * HALVES * GROUPS)
                nc.scalar.activation(bot_hi[:, par, :], xt[:, :, 0], ACT.Copy).then_inc(bot_hi_ready, 1)

            def h1_out(u):
                for n in range(N1):
                    act.wait_ge(layer1_done, u * N1 + n + 1)
                    nc.scalar.activation(h1_hi[:, n, :], layer[:, n % 2, 0:UNIT], ACT.Relu,
                                         bias=b1_sb[:, n:n + 1]).then_inc(h1_hi_ready, 1)

            def gram_out(u, h):
                act.wait_ge(gram_ready, u * HALVES + h + 1)
                for q in range(Q):
                    for r in range(Q):
                        nc.scalar.activation(pair_view(pair_hi, h, q, r), gram_view(h, q, r),
                                             ACT.Copy).then_inc(pair_hi_ready, 1)

            def h2_out(u):
                for m in range(N2):
                    act.wait_ge(layer2_done, u * N2 + m + 1)
                    nc.scalar.activation(h2_sb[:, m, :], layer[:, m % 2, 0:UNIT], ACT.Relu,
                                         bias=b2_sb[:, m:m + 1]).then_inc(h2_ready, 1)

            def y_row(u):
                if not first(u):
                    act.wait_ge(y_stored, u * 16)
                act.wait_ge(layer3_done, u + 1)
                nc.scalar.activation(y_sb[:, :], layer[0:1, 0, 0:UNIT], ACT.Copy).then_inc(y_ready, 1)

            def step(u, par):
                if not first(u):
                    act.wait_ge(gram_ready, u * HALVES)
                    act.wait_ge(bot_lo_ready, u)
                turned_out(u, par)
                if not first(u):
                    h1_out(u - 1)
                gram_out(u, 0)
                if not first(u):
                    h2_out(u - 1)
                gram_out(u, 1)
                if not first(u):
                    y_row(u - 1)

            over_units(act, step)
            h1_out(UNITS - 1)
            h2_out(UNITS - 1)
            y_row(UNITS - 1)

        @block.vector
        def _(dve):
            nc.vector.memset(w1_stage[:, 0:IN2 * H1], 0.0).then_inc(stage_zero, 1)
            nc.vector.memset(w1_rest, 0.0).then_inc(stage_zero, 1)
            nc.vector.memset(pair_hi[:, :, :].bitcast(f32), 0.0).then_inc(pad_zero, 1)
            nc.vector.memset(pair_lo[:, :, :].bitcast(f32), 0.0).then_inc(pad_zero, 1)

            def low(out, whole, high, n):
                dve.wait_ge(w_hi, n)
                return nc.vector.tensor_tensor(out, whole, high.bitcast(f32), ALU.subtract)

            low(w2_lo[:, :, :].rearrange("p k n -> p (k n)"), w2_stage,
                w2_hi[:, :, :].rearrange("p k n -> p (k n)"), 1)
            fl, fh = (w[:, :, :].rearrange("p c n -> p (c n)") for w in (w1_lo, w1_hi))
            low(fl[:, 0:IN2 * H1], w1_stage[:, 0:IN2 * H1], fh[:, 0:IN2 * H1], 2)
            low(fl[:, IN2 * H1:CH * H1], w1_rest, fh[:, IN2 * H1:CH * H1], 3)
            low(fl[:, CH * H1:], w1_bot_stage, fh[:, CH * H1:], 4).then_inc(w_split, 1)

            def h1_out(u):
                for n in range(N1):
                    dve.wait_ge(h1_hi_ready, u * N1 + n + 1)
                    if not (first(u) and n == 0):
                        dve.wait_ge(h1_lo_ready, u * N1 + n)
                    nc.vector.tensor_scalar(h1_f[:, :], layer[:, n % 2, 0:UNIT], b1_sb[:, n:n + 1], 0.0,
                                            ALU.add, ALU.max).then_inc(h1_f_ready, 1)
                    dve.wait_ge(h1_f_ready, u * N1 + n + 1)
                    nc.vector.tensor_tensor(h1_lo[:, n, :], h1_f[:, :], h1_hi[:, n, :].bitcast(f32),
                                            ALU.subtract).then_inc(h1_lo_ready, 1)

            def gram_out(u, h):
                for q in range(Q):
                    dve.wait_ge(pair_hi_ready, ((u * HALVES + h) * Q + q + 1) * Q)
                    for r in range(Q):
                        nc.vector.tensor_tensor(pair_view(pair_lo, h, q, r), gram_view(h, q, r),
                                                pair_view(pair_hi, h, q, r).bitcast(f32),
                                                ALU.subtract).then_inc(pair_lo_ready, 1)

            def step(u, par):
                dve.wait_ge(bot_hi_ready, u + 1)
                nc.vector.tensor_tensor(bot_lo[:, par, :], xt[:, :, 0], bot_hi[:, par, :].bitcast(f32),
                                        ALU.subtract).then_inc(bot_lo_ready, 1)
                if not first(u):
                    h1_out(u - 1)
                gram_out(u, 0)
                gram_out(u, 1)

            dve.wait_ge(small_in, 3 * 16)
            over_units(dve, step)
            h1_out(UNITS - 1)

        @block.tensor
        def _(pe):
            pe.wait_ge(ident_ready, 1)
            pe.wait_ge(pad_zero, 2)

            def turn(u, par):
                for h in range(HALVES):
                    s = par * HALVES + h
                    pe.wait_ge(bottom_in[s], (u - par) * 8 + 16)
                    for g in range(GROUPS):
                        n = h * GROUPS + g
                        fs = group(g)
                        if not (first(u) and n < 2):
                            pe.wait_ge(xt_ready, u * HALVES * GROUPS + n - 1)
                        tables_in = len([f for f in fs if f])
                        pe.wait_ge(gathered[s][g], ((u - par) * 8 + 16) * tables_in)
                        for k, f in enumerate(fs):
                            last = nc.tensor.transpose(turned[:, n % 2, k, :], emb[s][:, f, :], ident[:, :])
                        last.then_inc(turned_ready, 1)

            def three_passes(out, terms):
                n = 0
                for whi, wlo, xhi, xlo in terms:
                    for w, x in ((whi, xhi), (wlo, xhi), (whi, xlo)):
                        last = nc.tensor.matmul(out, w, x, start=(n == 0), stop=(n == 3 * len(terms) - 1))
                        n += 1
                return last

            def layer1(u, par):
                pe.wait_ge(pair_lo_ready, (u + 1) * HALVES * Q * Q)
                pe.wait_ge(bot_lo_ready, u + 1)
                if not first(u):
                    pe.wait_ge(h2_ready, u * N2)
                    pe.wait_ge(y_ready, u)
                for n in range(N1):
                    cols = slice(n * P, (n + 1) * P)
                    if n >= 2:
                        pe.wait_ge(h1_lo_ready, u * N1 + n - 1)
                    terms = [(w1_hi[:, c, cols], w1_lo[:, c, cols], pair_hi[:, c, :], pair_lo[:, c, :])
                             for c in range(CH)]
                    terms.append((w1_hi[:, CH, cols], w1_lo[:, CH, cols], bot_hi[:, par, :], bot_lo[:, par, :]))
                    three_passes(layer[:, n % 2, 0:UNIT], terms).then_inc(layer1_done, 1)

            def layer2(u):
                pe.wait_ge(h1_lo_ready, (u + 1) * N1)
                for m in range(N2):
                    cols = slice(m * P, (m + 1) * P)
                    terms = [(w2_hi[:, k, cols], w2_lo[:, k, cols], h1_hi[:, k, :], h1_lo[:, k, :])
                             for k in range(N1)]
                    three_passes(layer[:, m % 2, 0:UNIT], terms).then_inc(layer2_done, 1)

            def layer3(u):
                pe.wait_ge(h2_ready, (u + 1) * N2)
                for m in range(N2):
                    last = nc.tensor.matmul(layer[0:1, 0, 0:UNIT], w3_sb[:, m:m + 1], h2_sb[:, m, :],
                                            start=(m == 0), stop=(m == N2 - 1))
                last.then_inc(layer3_done, 1)

            def gram(u, h):
                pe.wait_ge(xt_ready, u * HALVES * GROUPS + (h + 1) * GROUPS)
                if not first(u):
                    pe.wait_ge(pair_lo_ready, ((u - 1) * HALVES + h + 1) * Q * Q)
                for x in range(QP):
                    for q in range(Q):
                        b = h * TILE + q * QP + x
                        at = x % XB * J
                        last = nc.tensor.matmul(
                            grams[QP * q:QP * q + J, 2 * h + x // XB, at:at + J],
                            xt[:, b, 0:J], xt[:, b, 1:F], start=True, stop=True)
                last.then_inc(gram_ready, 1)

            def step(u, par):
                turn(u, par)
                if first(u):
                    pe.wait_ge(w_split, 1)
                    pe.wait_ge(small_in, 3 * 16)
                else:
                    layer1(u - 1, 1 - par)
                gram(u, 0)
                if not first(u):
                    layer2(u - 1)
                gram(u, 1)
                if not first(u):
                    layer3(u - 1)

            over_units(pe, step)
            layer1(UNITS - 1, 1)
            layer2(UNITS - 1)
            layer3(UNITS - 1)


TABLE_COUNT = 26


def kernel(**inputs):
    import numpy as np
    import concourse.bacc as bacc
    from concourse.bass_utils import run_bass_kernel_spmd

    nc = bacc.Bacc("TRN2", target_bir_lowering=False, num_devices=1)
    arrays = {}

    def give(name, a):
        a = np.ascontiguousarray(a)
        arrays[name] = a
        return nc.dram_tensor(name, a.shape, mybir.dt.from_np(a.dtype), kind="ExternalInput").ap()

    def columns(a):
        return np.asarray(a).reshape(-1, 128).T

    bottom = give("bottom", inputs["r_bottom_output"])
    ids = give("ids", inputs["ids"])
    tables = [give(f"tbl_{i}", inputs[f"tbl_{i}"]) for i in range(TABLE_COUNT)]
    w1 = give("w_top1", inputs["W_top1"])
    b1 = give("b_top1", columns(inputs["b_top1"]))
    w2 = give("w_top2", inputs["W_top2"])
    b2 = give("b_top2", columns(inputs["b_top2"]))
    w3 = give("w_top3", columns(inputs["W_top3"]))
    y = nc.dram_tensor("y", (bottom.shape[0], 1), mybir.dt.float32, kind="ExternalOutput").ap()
    dlrm_tower(nc, bottom, ids, tables, w1, b1, w2, b2, w3, y)
    r = run_bass_kernel_spmd(nc, [arrays], core_ids=[0])
    return r.results[0]["y"]
```

```python
from contextlib import ExitStack

import concourse.bass as bass
from concourse import mybir

LOOKED_UP = 7


def choose_tables(rows):
    small = sorted(sorted(range(len(rows)), key=lambda t: (rows[t], t))[:LOOKED_UP])
    return [t for t in range(len(rows)) if t not in small], small


def pack_groups(places):
    wanted = {7: 24, 5: 18}
    groups, start = [], 0
    for k in range(places // 3):
        height = min(wanted.get(k, 3 * k + 2), places - 1)
        groups.append((start, height, [j for j in range(3 * k, 3 * k + 3) if j > 0]))
        start += height
    return groups


def pair_order(places, features):
    def row(i, j):
        a, b = sorted((features[i], features[j]))
        return a * places - a * (a + 1) // 2 + b - a - 1

    order = []
    for _, _, cols in pack_groups(places):
        for i in range(cols[-1]):
            order += [row(i, j) for j in cols if j > i]
    return order


def dlrm_tower(nc, bottom, ids, id_rows, tables, small_tables, w1, w1_bottom, b1, w2, b2, w3, y_out):
    f32, f32r, i32 = mybir.dt.float32, mybir.dt.float32r, mybir.dt.int32
    ACT = mybir.ActivationFunctionType
    ALU = mybir.AluOpType

    BATCH, D = bottom.shape
    P = 128
    TILE = P
    HALVES = 2
    UNIT = TILE * HALVES
    UNITS = BATCH // UNIT
    SLOTS = 2 * HALVES
    H1, H2 = w1.shape[1], w2.shape[1]
    N1, N2 = H1 // P, H2 // P

    GATHERED, K = len(tables), len(small_tables)
    E = GATHERED + 1
    PLACES = E + K
    FB = 4
    TURNS = -(-E // FB)
    EVAC = HALVES * TURNS + K
    J = PLACES - 1

    ROWS = small_tables[0].shape[0]
    RCH = 8
    RP = ROWS // RCH
    assert RP * RCH == ROWS and RP <= P and all(t.shape[0] == ROWS for t in small_tables)
    HOT = 4
    PIECES = K * RCH // HOT
    RING = 4
    AHEAD = 4
    assert (2 * PIECES) % RING == 0 and RCH == 2 * HOT

    Q = 4
    QP = P // Q
    XB = 16
    BANKS = UNIT // Q // XB
    QX = UNIT // Q
    GROUPS = pack_groups(PLACES)
    PACK = 3
    CHUNKS = PACK + 1
    assert sum(h for _, h, _ in GROUPS) == P
    PACKS = Q * len(GROUPS)

    ctx = ExitStack()
    with ctx:
        def sb(name, shape, dt):
            return ctx.enter_context(nc.sbuf_tensor(name, shape, dt))

        def pb(name, shape):
            return ctx.enter_context(nc.psum_tensor(name, shape, f32))

        def sem(name):
            return ctx.enter_context(nc.semaphore(name))

        emb = [sb(f"emb{s}", [P, E, D], f32) for s in range(SLOTS)]
        idx = [sb(f"idx{s}", [P, GATHERED], i32) for s in range(SLOTS)]
        xt = sb("xt", [P, UNIT, PLACES], f32)
        tab_hi = sb("tab_hi", [RP, K, RCH * D], f32r)
        tab_lo = sb("tab_lo", [RP, K, RCH * D], f32r)
        id_bc = sb("id_bc", [P, K, UNIT], i32)
        hot = sb("hot", [RP, RING, HOT, UNIT], f32r)
        row_i = sb("row_i", [P, RCH], i32)
        gram_hl = sb("gram_hl", [P, J, 2, QX], f32r)
        pairs = sb("pairs", [P, PACK, Q, 2, QX], f32r)
        bot_hi = sb("bot_hi", [P, UNIT], f32r)
        bot_lo = sb("bot_lo", [P, UNIT], f32r)
        w1_hi = sb("w1_hi", [P, CHUNKS, H1], f32r)
        w1_lo = sb("w1_lo", [P, CHUNKS, H1], f32r)
        w2_hi = sb("w2_hi", [P, N1, H2], f32r)
        w2_lo = sb("w2_lo", [P, N1, H2], f32r)
        w3_sb = sb("w3_sb", [P, N2], f32)
        b1_sb = sb("b1_sb", [P, N1], f32)
        b2_sb = sb("b2_sb", [P, N2], f32)
        h1_f = sb("h1_f", [P, UNIT], f32)
        h1_hi = sb("h1_hi", [P, N1, UNIT], f32r)
        h1_lo = sb("h1_lo", [P, N1, UNIT], f32r)
        h2_sb = sb("h2_sb", [P, N2, UNIT], f32)
        y_sb = sb("y_sb", [1, UNIT], f32)
        ident = sb("ident", [P, P], f32)

        def stage(tensor, at, width):
            flat = tensor[:, :, :].rearrange("p a b -> p (a b)")
            assert (at + width) * 4 <= tensor[:, :, :].free_nbytes()
            return flat[:, at:at + width]

        w1_stage = stage(emb[3], 0, PACK * H1)
        bottom_stage = stage(emb[3], PACK * H1, H1)
        w2_stage = stage(emb[2], 0, N1 * H2)
        in_xt = UNIT * PLACES // (RCH * D)
        tab_stage = [(stage(xt, t * RCH * D, RCH * D) if t < in_xt else
                      stage(emb[2], N1 * H2 + (t - in_xt) * RCH * D, RCH * D))[0:RP, :] for t in range(K)]

        turned = pb("turned", [P, 2, FB * P])
        grams = pb("grams", [P, 2, 512])
        layer = pb("layer", [P, 2, 512])
        row_of = pb("row_of", [P, 512])

        gathered = [[sem(f"gathered{s}_{g}") for g in range(TURNS)] for s in range(SLOTS)]
        idx_in = [sem(f"idx_in{s}") for s in range(SLOTS)]
        bottom_in = [sem(f"bottom_in{s}") for s in range(SLOTS)]
        stage_zero = sem("stage_zero")
        tab_in = [sem(f"tab_in{t}") for t in range(K)]
        w1_in = sem("w1_in")
        w2_in = sem("w2_in")
        small_in = sem("small_in")
        tab_hi_done = sem("tab_hi_done")
        tab_split = sem("tab_split")
        w_hi_done = sem("w_hi_done")
        w_split = sem("w_split")
        pad_zero = sem("pad_zero")
        ident_zero = sem("ident_zero")
        ident_ready = sem("ident_ready")
        rows_made = sem("rows_made")
        rows_ready = sem("rows_ready")
        tile_begun = sem("tile_begun")
        ids_in = sem("ids_in")
        hot_ready = sem("hot_ready")
        hot_first_used = sem("hot_first_used")
        turned_ready = sem("turned_ready")
        xt_ready = sem("xt_ready")
        bot_hi_ready = sem("bot_hi_ready")
        bot_lo_ready = sem("bot_lo_ready")
        gram_ready = sem("gram_ready")
        gram_hi_ready = sem("gram_hi_ready")
        gram_lo_ready = sem("gram_lo_ready")
        packed = sem("packed")
        layer1_done = sem("layer1_done")
        h1_hi_ready = sem("h1_hi_ready")
        h1_f_ready = sem("h1_f_ready")
        h1_lo_ready = sem("h1_lo_ready")
        layer2_done = sem("layer2_done")
        h2_ready = sem("h2_ready")
        layer3_done = sem("layer3_done")
        y_ready = sem("y_ready")
        y_stored = sem("y_stored")

        block = ctx.enter_context(nc.Block())

        def places_of(g):
            return range(g * FB, min((g + 1) * FB, E))

        ORDER = ([("turn", 0, g) for g in range(TURNS)] + [("look", None, t) for t in range(K)]
                 + [("turn", 1, g) for g in range(TURNS)])

        def over_units(engine, step, apart=1):
            pairs_of_units = (UNITS - 1 - apart) // 2
            step(0, 0)
            with engine.Fori(0, pairs_of_units) as v:
                step(v * 2 + 1, 1)
                step(v * 2 + 2, 0)
            for u in range(1 + 2 * pairs_of_units, UNITS):
                step(u, u % 2)

        def first(u):
            return isinstance(u, int) and u == 0

        def last_unit(u):
            return isinstance(u, int) and u == UNITS - 1

        def gram_bank(bank):
            src = grams[:, bank % 2, 0:XB * J].rearrange("p (x j) -> p j x", j=J)
            at = bank * XB
            return src, [gram_hl[:, :, part, at:at + XB] for part in range(2)]

        def send_packs(engine, quadrants):
            for q in quadrants:
                for start, height, cols in GROUPS:
                    c = PACK - len(cols)
                    engine.dma_start(
                        pairs[start:start + height, c:PACK, q, :, :].rearrange("p c l x -> p c (l x)").bitcast(f32),
                        gram_hl[q * QP:q * QP + height, cols[0] - 1:cols[-1], :, :]
                        .rearrange("p j l x -> p j (l x)").bitcast(f32),
                    ).then_inc(packed, 16)

        @block.sync
        def _(sp):
            def load_tile(t, s):
                sp.dma_start(idx[s][:, :], ids[bass.ds(t * TILE, TILE), :]).then_inc(idx_in[s], 16)
                sp.dma_start(emb[s][:, 0, :], bottom[bass.ds(t * TILE, TILE), :]).then_inc(bottom_in[s], 16)

            def load_ids(u):
                sp.dma_start(id_bc[:, :, :], id_rows[:, bass.ds(u * UNIT, UNIT)].partition_broadcast(P))\
                  .then_inc(ids_in, 16)

            load_tile(0, 0)
            load_ids(0)
            for t in range(K):
                sp.dma_start(tab_stage[t], small_tables[t].rearrange("(p c) d -> p (c d)", c=RCH))\
                  .then_inc(tab_in[t], 16)
            load_tile(1, 1)
            sp.wait_ge(stage_zero, 1)
            at = 0
            for start, _, cols in GROUPS:
                c0 = PACK - len(cols)
                whole, width = cols[0], len(cols)
                sp.dma_start(w1_stage[start:start + whole, c0 * H1:PACK * H1],
                             w1[at:at + whole * width, :].rearrange("(i c) n -> i (c n)", c=width))\
                  .then_inc(w1_in, 16)
                at += whole * width
                for i in range(cols[0], cols[-1]):
                    n = cols[-1] - i
                    sp.dma_start(w1_stage[start + i:start + i + 1, (PACK - n) * H1:PACK * H1],
                                 w1[at:at + n, :].rearrange("(a c) n -> a (c n)", a=1)).then_inc(w1_in, 16)
                    at += n
            sp.wait_ge(tab_split, K)
            sp.wait_ge(w_split, 1)
            load_tile(2, 2)
            sp.wait_ge(w_split, 2)
            load_tile(3, 3)

            def step(u, par):
                more = not isinstance(u, int) or u + 2 < UNITS
                if more:
                    sp.wait_ge(turned_ready, u * EVAC + TURNS)
                    load_tile((u + 2) * HALVES, par * HALVES)
                if not last_unit(u):
                    sp.wait_ge(hot_ready, (u + 1) * PIECES)
                    load_ids(u + 1)
                if more:
                    sp.wait_ge(turned_ready, (u + 1) * EVAC)
                    load_tile((u + 2) * HALVES + 1, par * HALVES + 1)
                sp.wait_ge(gram_lo_ready, (u + 1) * BANKS)
                send_packs(sp, range(Q))
                if not first(u):
                    store(u - 1)

            def store(u):
                sp.wait_ge(y_ready, u + 1)
                sp.dma_start(
                    y_out[bass.ds(u * UNIT, UNIT), :].rearrange("(h q x) c -> c q h x", h=HALVES, q=Q),
                    y_sb[:, :].rearrange("a (q h x) -> a q h x", q=Q, h=HALVES)).then_inc(y_stored, 16)

            over_units(sp, step, apart=3)
            store(UNITS - 1)
            sp.wait_ge(y_stored, UNITS * 16)

        @block.gpsimd
        def _(pool):
            pool.memset(ident[:, :], 0.0).then_inc(ident_zero, 1)
            pool.wait_ge(ident_zero, 1)
            pool.affine_select(out=ident[:, :], in_=ident[:, :], compare_op=ALU.not_equal, fill=1.0,
                               base=0, pattern=[[-1, P]], channel_multiplier=1).then_inc(ident_ready, 1)
            pool.iota(row_i[:, :], pattern=[[1, RCH]], base=0, channel_multiplier=RCH).then_inc(rows_made, 1)
            with pool.Fori(0, UNITS // 2) as v:
                for s in range(SLOTS):
                    pool.wait_ge(idx_in[s], (v + 1) * 16)
                    pool.sem_inc(tile_begun, 1)
                    for g in range(TURNS):
                        for e in places_of(g):
                            if e == 0:
                                continue
                            pool.indirect_dma_start(
                                emb[s][:, e, :], None, tables[e - 1],
                                bass.IndirectOffsetOnAxis(ap=idx[s][:, e - 1:e], axis=0),
                            ).then_inc(gathered[s][g], 16)

        @block.scalar
        def _(act):
            act.dma_start(w2_stage.rearrange("p (k n) -> p k n", k=N1),
                          w2.rearrange("(k p) n -> p k n", p=P)).then_inc(w2_in, 16)
            act.dma_start(bottom_stage, w1_bottom).then_inc(w1_in, 16)
            act.dma_start(b1_sb[:, :], b1).then_inc(small_in, 16)
            act.dma_start(b2_sb[:, :], b2).then_inc(small_in, 16)
            act.dma_start(w3_sb[:, :], w3).then_inc(small_in, 16)

            for t in range(K):
                act.wait_ge(tab_in[t], 16)
                nc.scalar.activation(tab_hi[:, t, :], tab_stage[t], ACT.Copy).then_inc(tab_hi_done, 1)
            act.wait_ge(w2_in, 16)
            nc.scalar.activation(w2_hi[:, :, :].rearrange("p k n -> p (k n)"), w2_stage,
                                 ACT.Copy).then_inc(w_hi_done, 1)

            def w1_high():
                act.wait_ge(w1_in, (1 + sum(len(cols) for _, _, cols in GROUPS)) * 16)
                nc.scalar.activation(w1_hi[:, 0:PACK, :].rearrange("p c n -> p (c n)"), w1_stage,
                                     ACT.Copy).then_inc(w_hi_done, 1)
                nc.scalar.activation(w1_hi[:, PACK, :], bottom_stage, ACT.Copy).then_inc(w_hi_done, 1)
                act.wait_ge(small_in, 3 * 16)

            def to_xt(u, par):
                for n, (kind, h, k) in enumerate(ORDER):
                    if first(u) and n == 0:
                        act.wait_ge(tab_split, K)
                    act.wait_ge(turned_ready, u * EVAC + n + 1)
                    src = turned[:, (par * EVAC + n) % 2, :]
                    if kind == "turn":
                        e = places_of(k)
                        dst = xt[:, h * TILE:(h + 1) * TILE, e[0]:e[-1] + 1]
                        src = src[:, 0:len(e) * P].rearrange("p (e b) -> p b e", b=P)
                    else:
                        dst, src = xt[:, :, E + k], src[:, 0:UNIT]
                    nc.scalar.activation(dst, src, ACT.Copy).then_inc(xt_ready, 1)

            def gram_high(u, bank):
                act.wait_ge(gram_ready, u * BANKS + bank + 1)
                src, (hi, _) = gram_bank(bank)
                nc.scalar.activation(hi, src, ACT.Copy).then_inc(gram_hi_ready, 1)

            def bottom_high(u):
                act.wait_ge(gram_ready, u * BANKS + 3)
                nc.scalar.activation(
                    bot_hi[:, :].rearrange("p (q h x) -> p q h x", q=Q, h=HALVES),
                    xt[:, :, 0].rearrange("p (h q x) -> p q h x", q=Q, h=HALVES),
                    ACT.Copy).then_inc(bot_hi_ready, 1)

            def h1_high(u):
                for n in range(N1):
                    act.wait_ge(layer1_done, u * N1 + n + 1)
                    nc.scalar.activation(h1_hi[:, n, :], layer[:, n % 2, 0:UNIT], ACT.Relu,
                                         bias=b1_sb[:, n:n + 1]).then_inc(h1_hi_ready, 1)

            def h2_out(u):
                for m in range(N2):
                    act.wait_ge(layer2_done, u * N2 + m + 1)
                    nc.scalar.activation(h2_sb[:, m, :], layer[:, m % 2, 0:UNIT], ACT.Relu,
                                         bias=b2_sb[:, m:m + 1]).then_inc(h2_ready, 1)

            def y_row(u):
                if not first(u):
                    act.wait_ge(y_stored, u * 16)
                act.wait_ge(layer3_done, u + 1)
                nc.scalar.activation(y_sb[:, :], layer[0:1, 0, 0:UNIT], ACT.Copy).then_inc(y_ready, 1)

            def step(u, par):
                if not first(u):
                    act.wait_ge(gram_ready, u * BANKS)
                    act.wait_ge(bot_lo_ready, u)
                to_xt(u, par)
                if first(u):
                    w1_high()
                else:
                    act.wait_ge(packed, u * PACKS * 16)
                gram_high(u, 0)
                gram_high(u, 1)
                if not first(u):
                    h1_high(u - 1)
                gram_high(u, 2)
                bottom_high(u)
                if not first(u):
                    h2_out(u - 1)
                gram_high(u, 3)
                if not first(u):
                    y_row(u - 1)

            over_units(act, step)
            h1_high(UNITS - 1)
            h2_out(UNITS - 1)
            y_row(UNITS - 1)

        @block.vector
        def _(dve):
            nc.vector.memset(w1_stage, 0.0).then_inc(stage_zero, 1)
            nc.vector.memset(pairs[:, :, :, :, :].rearrange("p c q l x -> p (c q l x)").bitcast(f32), 0.0).then_inc(pad_zero, 1)
            nc.vector.memset(grams[:, 0, :], 0.0).then_inc(pad_zero, 1)
            nc.vector.memset(grams[:, 1, :], 0.0).then_inc(pad_zero, 1)
            dve.wait_ge(rows_made, 1)
            nc.vector.tensor_copy(row_of[:, 0:RCH], row_i[:, :]).then_inc(rows_ready, 1)
            dve.wait_ge(rows_ready, 1)

            def one_hot(u, n, turn):
                t, c = n * HOT // RCH, n * HOT % RCH
                old = t - RING // 2
                if not (first(u) and old < 0):
                    if c == 0:
                        dve.wait_ge(hot_first_used, u * K + old + 1)
                    elif old >= 0:
                        dve.wait_ge(turned_ready, u * EVAC + TURNS + old + 1)
                    else:
                        dve.wait_ge(turned_ready, (u - 1) * EVAC + TURNS + K + old + 1)
                nc.vector.tensor_tensor(
                    hot[:, turn, :, :],
                    id_bc[0:RP, t, :].unsqueeze(1).broadcast_to([RP, HOT, UNIT]),
                    row_of[0:RP, c:c + HOT].unsqueeze(2).broadcast_to([RP, HOT, UNIT]),
                    ALU.is_equal).then_inc(hot_ready, 1)

            for t in range(K):
                dve.wait_ge(tab_hi_done, t + 1)
                nc.vector.tensor_tensor(tab_lo[:, t, :], tab_stage[t], tab_hi[:, t, :].bitcast(f32),
                                        ALU.subtract).then_inc(tab_split, 1)
            dve.wait_ge(w_hi_done, 1)
            nc.vector.tensor_tensor(
                w2_lo[:, :, :].rearrange("p k n -> p (k n)"), w2_stage,
                w2_hi[:, :, :].rearrange("p k n -> p (k n)").bitcast(f32), ALU.subtract).then_inc(w_split, 1)

            def w1_low():
                dve.wait_ge(w_hi_done, 3)
                nc.vector.tensor_tensor(
                    w1_lo[:, 0:PACK, :].rearrange("p c n -> p (c n)"), w1_stage,
                    w1_hi[:, 0:PACK, :].rearrange("p c n -> p (c n)").bitcast(f32), ALU.subtract)
                nc.vector.tensor_tensor(w1_lo[:, PACK, :], bottom_stage, w1_hi[:, PACK, :].bitcast(f32),
                                        ALU.subtract).then_inc(w_split, 1)
                dve.wait_ge(small_in, 3 * 16)

            def gram_low(u, bank):
                dve.wait_ge(gram_hi_ready, u * BANKS + bank + 1)
                src, (hi, lo) = gram_bank(bank)
                nc.vector.tensor_tensor(lo, src, hi.bitcast(f32), ALU.subtract).then_inc(gram_lo_ready, 1)

            def bottom_low(u):
                dve.wait_ge(bot_hi_ready, u + 1)
                nc.vector.tensor_tensor(
                    bot_lo[:, :].rearrange("p (q h x) -> p q h x", q=Q, h=HALVES),
                    xt[:, :, 0].rearrange("p (h q x) -> p q h x", q=Q, h=HALVES),
                    bot_hi[:, :].rearrange("p (q h x) -> p q h x", q=Q, h=HALVES).bitcast(f32),
                    ALU.subtract).then_inc(bot_lo_ready, 1)

            def h1_low(u):
                for n in range(N1):
                    dve.wait_ge(h1_hi_ready, u * N1 + n + 1)
                    if not (first(u) and n == 0):
                        dve.wait_ge(h1_lo_ready, u * N1 + n)
                    nc.vector.tensor_scalar(h1_f[:, :], layer[:, n % 2, 0:UNIT], b1_sb[:, n:n + 1], 0.0,
                                            ALU.add, ALU.max).then_inc(h1_f_ready, 1)
                    dve.wait_ge(h1_f_ready, u * N1 + n + 1)
                    nc.vector.tensor_tensor(h1_lo[:, n, :], h1_f[:, :], h1_hi[:, n, :].bitcast(f32),
                                            ALU.subtract).then_inc(h1_lo_ready, 1)

            def step(u, par):
                for n in range(0 if first(u) else AHEAD, PIECES):
                    if first(u) and n == 0:
                        dve.wait_ge(ids_in, 16)
                    one_hot(u, n, (par * PIECES + n) % RING)
                if first(u):
                    w1_low()
                gram_low(u, 0)
                gram_low(u, 1)
                if not first(u):
                    h1_low(u - 1)
                if not last_unit(u):
                    dve.wait_ge(ids_in, (u + 2) * 16)
                    for n in range(AHEAD // 2):
                        one_hot(u + 1, n, ((1 - par) * PIECES + n) % RING)
                gram_low(u, 2)
                bottom_low(u)
                if not last_unit(u):
                    for n in range(AHEAD // 2, AHEAD):
                        one_hot(u + 1, n, ((1 - par) * PIECES + n) % RING)
                gram_low(u, 3)

            over_units(dve, step)
            h1_low(UNITS - 1)

        @block.tensor
        def _(pe):
            pe.wait_ge(ident_ready, 1)
            pe.wait_ge(pad_zero, 3)

            def turn(u, par, n, h, g):
                s = par * HALVES + h
                if g == 0:
                    pe.wait_ge(bottom_in[s], (u - par) * 8 + 16)
                e = places_of(g)
                pe.wait_ge(gathered[s][g], ((u - par) * 8 + 16) * len([x for x in e if x]))
                for k, place in enumerate(e):
                    last = nc.tensor.transpose(turned[:, (par * EVAC + n) % 2, k * P:(k + 1) * P],
                                               emb[s][:, place, :], ident[:, :])
                last.then_inc(turned_ready, 1)

            def look_up(u, par, n, t):
                out = turned[:, (par * EVAC + n) % 2, 0:UNIT]
                if first(u):
                    pe.wait_ge(tab_split, t + 1)
                for c in range(RCH):
                    piece = (t * RCH + c) // HOT
                    if c % HOT == 0:
                        pe.wait_ge(hot_ready, u * PIECES + piece + 1)
                    for tab in (tab_hi, tab_lo):
                        last = nc.tensor.matmul(
                            out, tab[:, t, c * D:(c + 1) * D],
                            hot[:, (par * PIECES + piece) % RING, c % HOT, :],
                            start=(c == 0 and tab is tab_hi), stop=(c == RCH - 1 and tab is tab_lo))
                    if c % HOT == HOT - 1 and c < RCH - 1:
                        last.then_inc(hot_first_used, 1)
                return last

            def three_passes(out, terms):
                n = 0
                for whi, wlo, xhi, xlo in terms:
                    for w, x in ((whi, xhi), (wlo, xhi), (whi, xlo)):
                        last = nc.tensor.matmul(out, w, x, start=(n == 0), stop=(n == 3 * len(terms) - 1))
                        n += 1
                return last

            def layer1(u):
                pe.wait_ge(packed, (u + 1) * PACKS * 16)
                pe.wait_ge(bot_lo_ready, u + 1)
                if not first(u):
                    pe.wait_ge(y_ready, u)
                for n in range(N1):
                    cols = slice(n * P, (n + 1) * P)
                    if n >= 2:
                        pe.wait_ge(h1_lo_ready, u * N1 + n - 1)
                    terms = [(w1_hi[:, c, cols], w1_lo[:, c, cols], pairs[:, c, :, 0, :], pairs[:, c, :, 1, :])
                             for c in range(PACK)]
                    terms.append((w1_hi[:, PACK, cols], w1_lo[:, PACK, cols], bot_hi[:, :], bot_lo[:, :]))
                    three_passes(layer[:, n % 2, 0:UNIT], terms).then_inc(layer1_done, 1)

            def layer2(u):
                pe.wait_ge(h1_lo_ready, (u + 1) * N1)
                for m in range(N2):
                    cols = slice(m * P, (m + 1) * P)
                    terms = [(w2_hi[:, k, cols], w2_lo[:, k, cols], h1_hi[:, k, :], h1_lo[:, k, :])
                             for k in range(N1)]
                    three_passes(layer[:, m % 2, 0:UNIT], terms).then_inc(layer2_done, 1)

            def layer3(u):
                pe.wait_ge(h2_ready, (u + 1) * N2)
                for m in range(N2):
                    last = nc.tensor.matmul(layer[0:1, 0, 0:UNIT], w3_sb[:, m:m + 1], h2_sb[:, m, :],
                                            start=(m == 0), stop=(m == N2 - 1))
                last.then_inc(layer3_done, 1)

            def gram(u, bank):
                h, x0 = bank * XB // QP, bank * XB % QP
                if not first(u) or bank >= 2:
                    pe.wait_ge(gram_lo_ready, u * BANKS + bank - 1)
                for x in range(XB):
                    for q in range(Q):
                        b = h * TILE + q * QP + x0 + x
                        last = nc.tensor.matmul(
                            grams[QP * q:QP * q + J, bank % 2, x * J:(x + 1) * J],
                            xt[:, b, 0:J], xt[:, b, 1:PLACES], start=True, stop=True)
                last.then_inc(gram_ready, 1)

            def step(u, par):
                for n, (kind, h, k) in enumerate(ORDER):
                    if not (first(u) and n < 2):
                        pe.wait_ge(xt_ready, u * EVAC + n - 1)
                    if kind == "turn":
                        turn(u, par, n, h, k)
                    else:
                        look_up(u, par, n, k).then_inc(turned_ready, 1)
                pe.wait_ge(xt_ready, (u + 1) * EVAC)
                gram(u, 0)
                gram(u, 1)
                if first(u):
                    pe.wait_ge(w_split, 2)
                    pe.wait_ge(small_in, 3 * 16)
                else:
                    layer1(u - 1)
                gram(u, 2)
                if not first(u):
                    layer2(u - 1)
                gram(u, 3)
                if not first(u):
                    layer3(u - 1)

            over_units(pe, step)
            layer1(UNITS - 1)
            layer2(UNITS - 1)
            layer3(UNITS - 1)


TABLES = 26


def kernel(**inputs):
    import numpy as np
    import concourse.bacc as bacc
    from concourse.bass_utils import run_bass_kernel_spmd

    nc = bacc.Bacc("TRN2", target_bir_lowering=False, num_devices=1)
    arrays = {}

    def give(name, a):
        a = np.ascontiguousarray(a)
        arrays[name] = a
        return nc.dram_tensor(name, a.shape, mybir.dt.from_np(a.dtype), kind="ExternalInput").ap()

    def columns(a):
        return np.asarray(a).reshape(-1, 128).T

    large, small = choose_tables([inputs[f"tbl_{t}"].shape[0] for t in range(TABLES)])
    features = [0] + [t + 1 for t in large + small]
    places = len(features)
    order = pair_order(places, features)

    ids, w1 = np.asarray(inputs["ids"]), np.asarray(inputs["W_top1"])
    bottom = give("bottom", inputs["r_bottom_output"])
    y = nc.dram_tensor("y", (bottom.shape[0], 1), mybir.dt.float32, kind="ExternalOutput").ap()
    dlrm_tower(
        nc, bottom,
        give("ids_large", ids[:, large]),
        give("ids_small", ids[:, small].T),
        [give(f"tbl_{t}", inputs[f"tbl_{t}"]) for t in large],
        [give(f"tbl_{t}", inputs[f"tbl_{t}"]) for t in small],
        give("w1_pairs", w1[order]),
        give("w1_bottom", w1[len(order):]),
        give("b_top1", columns(inputs["b_top1"])),
        give("w_top2", inputs["W_top2"]),
        give("b_top2", columns(inputs["b_top2"])),
        give("w_top3", columns(inputs["W_top3"])),
        y)
    r = run_bass_kernel_spmd(nc, [arrays], core_ids=[0])
    return r.results[0]["y"]
```

```python
from contextlib import ExitStack

import concourse.bass as bass
from concourse import mybir

LOOKED_UP = 8


def choose_tables(rows):
    small = sorted(sorted(range(len(rows)), key=lambda t: (rows[t], t))[:LOOKED_UP])
    return [t for t in range(len(rows)) if t not in small], small


def pack_groups(places):
    wanted = {7: 24, 5: 18}
    groups, start = [], 0
    for k in range(places // 3):
        height = min(wanted.get(k, 3 * k + 2), places - 1)
        groups.append((start, height, [j for j in range(3 * k, 3 * k + 3) if j > 0]))
        start += height
    return groups


def pair_order(places, features):
    def row(i, j):
        a, b = sorted((features[i], features[j]))
        return a * places - a * (a + 1) // 2 + b - a - 1

    order = []
    for _, _, cols in pack_groups(places):
        for i in range(cols[-1]):
            order += [row(i, j) for j in cols if j > i]
    return order


def dlrm_tower(nc, bottom, ids, id_rows, tables, small_tables, w1, w1_bottom, b1, w2, b2, w3, y_out):
    f32, f32r, i32 = mybir.dt.float32, mybir.dt.float32r, mybir.dt.int32
    ACT = mybir.ActivationFunctionType
    ALU = mybir.AluOpType

    BATCH, D = bottom.shape
    P = 128
    TILE = P
    HALVES = 2
    UNIT = TILE * HALVES
    UNITS = BATCH // UNIT
    SLOTS = 2 * HALVES
    H1, H2 = w1.shape[1], w2.shape[1]
    N1, N2 = H1 // P, H2 // P

    GATHERED, K = len(tables), len(small_tables)
    E = GATHERED + 1
    PLACES = E + K
    FB = 4
    TURNS = -(-E // FB)
    EVAC = HALVES * TURNS + K
    J = PLACES - 1

    ROWS = small_tables[0].shape[0]
    RCH = 8
    RP = ROWS // RCH
    assert RP * RCH == ROWS and RP <= P and all(t.shape[0] == ROWS for t in small_tables)
    HOT = 4
    PIECES = K * RCH // HOT
    RING = 4
    assert RCH == 2 * HOT and PIECES % RING == 0

    Q = 4
    QP = P // Q
    XB = 16
    BANKS = UNIT // Q // XB
    QX = UNIT // Q
    GROUPS = pack_groups(PLACES)
    PACK = 3
    CHUNKS = PACK + 1
    assert sum(h for _, h, _ in GROUPS) == P
    TURNED = 3
    assert EVAC % TURNED == 0

    ctx = ExitStack()
    with ctx:
        def sb(name, shape, dt):
            return ctx.enter_context(nc.sbuf_tensor(name, shape, dt))

        def pb(name, shape):
            return ctx.enter_context(nc.psum_tensor(name, shape, f32))

        def sem(name):
            return ctx.enter_context(nc.semaphore(name))

        emb = [sb(f"emb{s}", [P, E, D], f32) for s in range(SLOTS)]
        idx = [sb(f"idx{s}", [P, GATHERED], i32) for s in range(SLOTS)]
        xt = sb("xt", [P, UNIT, PLACES], f32)
        tab_hi = sb("tab_hi", [RP, K, RCH * D], f32r)
        tab_lo = sb("tab_lo", [RP, K, RCH * D], f32r)
        id_bc = sb("id_bc", [P, K, UNIT], i32)
        hot = sb("hot", [RP, RING, HOT, UNIT], f32r)
        row_i = sb("row_i", [P, RCH], i32)
        gram_sb = sb("gram_sb", [P, J, QX], f32)
        pairs = sb("pairs", [P, Q, PACK, QX], f32)
        pairs_hi = sb("pairs_hi", [P, PACK, UNIT], f32r)
        pairs_lo = sb("pairs_lo", [P, PACK, UNIT], f32r)
        bot_hi = sb("bot_hi", [P, UNIT], f32r)
        bot_lo = sb("bot_lo", [P, UNIT], f32r)
        w1_hi = sb("w1_hi", [P, CHUNKS, H1], f32r)
        w1_lo = sb("w1_lo", [P, CHUNKS, H1], f32r)
        w2_hi = sb("w2_hi", [P, N1, H2], f32r)
        w2_lo = sb("w2_lo", [P, N1, H2], f32r)
        w3_sb = sb("w3_sb", [P, N2], f32)
        b1_sb = sb("b1_sb", [P, N1], f32)
        b2_sb = sb("b2_sb", [P, N2], f32)
        h1_f = sb("h1_f", [P, 2, UNIT], f32)
        h1_hi = sb("h1_hi", [P, N1, UNIT], f32r)
        h1_lo = sb("h1_lo", [P, N1, UNIT], f32r)
        h2_sb = sb("h2_sb", [P, N2, UNIT], f32)
        y_sb = h2_sb[0:1, 0, :]
        ident = sb("ident", [P, P], f32)

        def stage(tensor, at, width):
            flat = tensor[:, :, :].rearrange("p a b -> p (a b)")
            assert (at + width) * 4 <= tensor[:, :, :].free_nbytes()
            return flat[:, at:at + width]

        w1_stage = stage(emb[3], 0, PACK * H1)
        bottom_stage = stage(emb[3], PACK * H1, H1)
        w2_stage = stage(emb[2], 0, N1 * H2)
        spots = ([stage(emb[1], 0, RCH * D), stage(emb[2], N1 * H2, RCH * D)]
                 + [stage(xt, n * RCH * D, RCH * D) for n in range(K - 2)])
        tab_stage = [spot[0:RP, :] for spot in spots]

        turned = pb("turned", [P, TURNED, FB * P])
        grams = pb("grams", [P, 2, 512])
        layer = pb("layer", [P, 2, 512])
        row_of = pb("row_of", [P, 512])

        gathered = [[sem(f"gathered{s}_{g}") for g in range(TURNS)] for s in range(SLOTS)]
        idx_in = [sem(f"idx_in{s}") for s in range(SLOTS)]
        bottom_in = [sem(f"bottom_in{s}") for s in range(SLOTS)]
        stage_zero = sem("stage_zero")
        tab_in = [sem(f"tab_in{t}") for t in range(K)]
        w1_in = sem("w1_in")
        w2_in = sem("w2_in")
        small_in = sem("small_in")
        tab_hi_done = sem("tab_hi_done")
        tab_split = sem("tab_split")
        w_hi_done = sem("w_hi_done")
        w_split = sem("w_split")
        pad_zero = sem("pad_zero")
        ident_zero = sem("ident_zero")
        ident_ready = sem("ident_ready")
        rows_made = sem("rows_made")
        rows_ready = sem("rows_ready")
        tile_begun = sem("tile_begun")
        ids_in = sem("ids_in")
        hot_ready = sem("hot_ready")
        hot_first_used = sem("hot_first_used")
        turned_ready = sem("turned_ready")
        looked_up = sem("looked_up")
        xt_ready = sem("xt_ready")
        bot_hi_ready = sem("bot_hi_ready")
        bot_lo_ready = sem("bot_lo_ready")
        gram_ready = sem("gram_ready")
        gram_out = [sem("gram_out_by_scalar"), sem("gram_out_by_vector")]
        packed = [sem(f"packed{half}") for half in range(2)]
        packed_by_pool = [sem(f"packed_by_pool{half}") for half in range(2)]
        pairs_hi_ready = sem("pairs_hi_ready")
        pairs_lo_ready = sem("pairs_lo_ready")
        layer1_done = sem("layer1_done")
        h1_hi_ready = sem("h1_hi_ready")
        h1_f_ready = sem("h1_f_ready")
        h1_lo_ready = sem("h1_lo_ready")
        layer2_done = sem("layer2_done")
        h2_ready = sem("h2_ready")
        layer3_done = sem("layer3_done")
        y_ready = sem("y_ready")
        y_stored = sem("y_stored")
        y_free = sem("y_free")

        block = ctx.enter_context(nc.Block())

        def places_of(g):
            return range(g * FB, min((g + 1) * FB, E))

        def first(u):
            return isinstance(u, int) and u == 0

        def last_unit(u):
            return isinstance(u, int) and u == UNITS - 1

        LOOKS = [("look", None, t) for t in range(K)]
        TURN0, TURN1 = ([("turn", h, g) for g in range(TURNS)] for h in range(HALVES))
        ITEMS = []
        for n in range(K):
            ITEMS.append(LOOKS[n])
            if n < TURNS:
                ITEMS.append(TURN0[n])
            else:
                ITEMS += TURN1[2 * (n - TURNS):2 * (n - TURNS) + 2]
        AHEAD = 5
        EARLY = [item for item in ITEMS if item not in TURN1]

        def over_units(engine, step, apart=1):
            pairs_of_units = (UNITS - 1 - apart) // 2
            step(0, 0)
            with engine.Fori(0, pairs_of_units) as v:
                step(v * 2 + 1, 1)
                step(v * 2 + 2, 0)
            for u in range(1 + 2 * pairs_of_units, UNITS):
                step(u, u % 2)

        def fills_of(u):
            if not last_unit(u):
                return [(range(Q), n * XB) for n in range(BANKS)]
            return [(tiles, n * XB) for tiles in (range(0, Q // 2), range(Q // 2, Q)) for n in range(BANKS)]

        def copy_gram(engine, copy, u, n):
            tiles, at = fills_of(u)[n]
            rows = slice(tiles[0] * QP, (tiles[-1] + 1) * QP)
            engine.wait_ge(gram_ready, u * BANKS + n + 1)
            copy(gram_sb[rows, :, at:at + XB],
                 grams[rows, n % 2, 0:XB * J].rearrange("p (x j) -> p j x", j=J)).then_inc(gram_out[n % 2], 1)

        PACKS = [[(group, q) for group in GROUPS for q in tiles] for tiles in ((0, 1), (2, 3))]
        POOL_PACKS = [[p for k, p in enumerate(packs) if k % 5 in (1, 3)] for packs in PACKS]

        def send_packs(engine, packs, done):
            for (start, height, cols), q in packs:
                engine.dma_start(
                    pairs[start:start + height, q, PACK - len(cols):PACK, :].rearrange("p c x -> p (c x)"),
                    gram_sb[q * QP:q * QP + height, cols[0] - 1:cols[-1], :].rearrange("p j x -> p (j x)"),
                ).then_inc(done, 16)

        def all_packed(engine, u):
            for half in range(2):
                by_pool = len(POOL_PACKS[half]) * 16 if last_unit(u) else 0
                engine.wait_ge(packed[half], (u + 1) * len(PACKS[half]) * 16 - by_pool)
                if by_pool:
                    engine.wait_ge(packed_by_pool[half], by_pool)

        @block.sync
        def _(sp):
            def load_tile(t, s):
                sp.dma_start(idx[s][:, :], ids[bass.ds(t * TILE, TILE), :]).then_inc(idx_in[s], 16)
                sp.dma_start(emb[s][:, 0, :], bottom[bass.ds(t * TILE, TILE), :]).then_inc(bottom_in[s], 16)

            sp.sem_inc(y_free, 1)
            load_tile(0, 0)
            sp.dma_start(id_bc[:, :, :], id_rows[:, 0:UNIT].partition_broadcast(P)).then_inc(ids_in, 16)
            for t in range(K):
                sp.dma_start(tab_stage[t], small_tables[t].rearrange("(p c) d -> p (c d)", c=RCH))\
                  .then_inc(tab_in[t], 16)
            sp.dma_start(w2_stage.rearrange("p (k n) -> p k n", k=N1),
                         w2.rearrange("(k p) n -> p k n", p=P)).then_inc(w2_in, 16)
            sp.dma_start(bottom_stage, w1_bottom).then_inc(w1_in, 16)
            sp.dma_start(b1_sb[:, :], b1).then_inc(small_in, 16)
            sp.dma_start(b2_sb[:, :], b2).then_inc(small_in, 16)
            sp.dma_start(w3_sb[:, :], w3).then_inc(small_in, 16)
            sp.wait_ge(tab_split, 1)
            load_tile(1, 1)
            sp.wait_ge(stage_zero, 1)
            at = 0
            for start, _, cols in GROUPS:
                c0 = PACK - len(cols)
                whole, width = cols[0], len(cols)
                sp.dma_start(w1_stage[start:start + whole, c0 * H1:PACK * H1],
                             w1[at:at + whole * width, :].rearrange("(i c) n -> i (c n)", c=width))\
                  .then_inc(w1_in, 16)
                at += whole * width
                for i in range(whole, cols[-1]):
                    n = cols[-1] - i
                    sp.dma_start(w1_stage[start + i:start + i + 1, (PACK - n) * H1:PACK * H1],
                                 w1[at:at + n, :].rearrange("(a c) n -> a (c n)", a=1)).then_inc(w1_in, 16)
                    at += n
            sp.wait_ge(tab_split, K)
            sp.wait_ge(w_split, 1)
            load_tile(2, 2)
            sp.wait_ge(w_split, 2)
            load_tile(3, 3)

            def step(u, par):
                more = not isinstance(u, int) or u + 2 < UNITS
                if more:
                    sp.wait_ge(turned_ready, u * HALVES * TURNS + TURNS)
                    load_tile((u + 2) * HALVES, par * HALVES)
                    sp.wait_ge(turned_ready, (u + 1) * HALVES * TURNS)
                    load_tile((u + 2) * HALVES + 1, par * HALVES + 1)
                if not first(u):
                    sp.wait_ge(pairs_lo_ready, u * PACK)
                for half in range(2):
                    if half == 0 or last_unit(u):
                        for by in gram_out:
                            sp.wait_ge(by, (u + 1 + half) * (BANKS // 2))
                    send_packs(sp, [p for p in PACKS[half] if not (last_unit(u) and p in POOL_PACKS[half])],
                               packed[half])
                if not first(u):
                    store(u - 1)

            def store(u):
                sp.wait_ge(y_ready, u + 1)
                sp.dma_start(y_out[bass.ds(u * UNIT, UNIT), :].rearrange("b c -> c b"), y_sb)\
                  .then_inc(y_stored, 16)
                sp.wait_ge(y_stored, (u + 1) * 16)
                sp.sem_inc(y_free, 1)

            over_units(sp, step, apart=3)
            store(UNITS - 1)

        @block.gpsimd
        def _(pool):
            pool.memset(ident[:, :], 0.0).then_inc(ident_zero, 1)
            pool.wait_ge(ident_zero, 1)
            pool.affine_select(out=ident[:, :], in_=ident[:, :], compare_op=ALU.not_equal, fill=1.0,
                               base=0, pattern=[[-1, P]], channel_multiplier=1).then_inc(ident_ready, 1)
            pool.iota(row_i[:, :], pattern=[[1, RCH]], base=0, channel_multiplier=RCH).then_inc(rows_made, 1)
            with pool.Fori(0, UNITS // 2) as v:
                for s in range(SLOTS):
                    pool.wait_ge(idx_in[s], (v + 1) * 16)
                    pool.sem_inc(tile_begun, 1)
                    for g in range(TURNS):
                        for e in places_of(g):
                            if e == 0:
                                continue
                            pool.indirect_dma_start(
                                emb[s][:, e, :], None, tables[e - 1],
                                bass.IndirectOffsetOnAxis(ap=idx[s][:, e - 1:e], axis=0),
                            ).then_inc(gathered[s][g], 16)
            pool.wait_ge(pairs_lo_ready, (UNITS - 1) * PACK)
            for half in range(2):
                for by in gram_out:
                    pool.wait_ge(by, (UNITS + half) * (BANKS // 2))
                send_packs(pool, POOL_PACKS[half], packed_by_pool[half])

        @block.scalar
        def _(act):
            for t in range(K):
                act.wait_ge(tab_in[t], 16)
                nc.scalar.activation(tab_hi[:, t, :], tab_stage[t], ACT.Copy).then_inc(tab_hi_done, 1)
            act.wait_ge(w2_in, 16)
            nc.scalar.activation(w2_hi[:, :, :].rearrange("p k n -> p (k n)"), w2_stage,
                                 ACT.Copy).then_inc(w_hi_done, 1)

            def w1_high():
                act.wait_ge(w1_in, (1 + sum(len(cols) for _, _, cols in GROUPS)) * 16)
                nc.scalar.activation(w1_hi[:, 0:PACK, :].rearrange("p c n -> p (c n)"), w1_stage,
                                     ACT.Copy).then_inc(w_hi_done, 1)
                nc.scalar.activation(w1_hi[:, PACK, :], bottom_stage, ACT.Copy).then_inc(w_hi_done, 1)
                act.wait_ge(small_in, 3 * 16)

            def to_xt(u, n, item):
                kind, h, k = item
                src = turned[:, n % TURNED, :]
                if kind == "turn":
                    act.wait_ge(turned_ready, (u * HALVES + h) * TURNS + k + 1)
                    e = places_of(k)
                    dst = xt[:, h * TILE:(h + 1) * TILE, e[0]:e[-1] + 1]
                    src = src[:, 0:len(e) * P].rearrange("p (e b) -> p b e", b=P)
                else:
                    act.wait_ge(looked_up, u * K + k + 1)
                    dst, src = xt[:, :, E + k], src[:, 0:UNIT]
                nc.scalar.activation(dst, src, ACT.Copy).then_inc(xt_ready, 1)

            def next_ids(u):
                act.wait_ge(hot_ready, (u + 1) * PIECES)
                act.dma_start(id_bc[:, :, :], id_rows[:, bass.ds((u + 1) * UNIT, UNIT)].partition_broadcast(P))\
                   .then_inc(ids_in, 16)

            def gram_copies(u, fills):
                for n in fills:
                    copy_gram(act, lambda out, x: nc.scalar.activation(out, x, ACT.Copy), u, n)

            def pairs_high(u):
                all_packed(act, u)
                for c in range(PACK):
                    nc.scalar.activation(pairs_hi[:, c, :].rearrange("p (q x) -> p q x", q=Q), pairs[:, :, c, :],
                                         ACT.Copy).then_inc(pairs_hi_ready, 1)

            def bottom_high(u):
                if not first(u):
                    act.wait_ge(layer1_done, u * N1)
                nc.scalar.activation(bot_hi[:, :], xt[:, :, 0], ACT.Copy).then_inc(bot_hi_ready, 1)

            def h1_high(u, parts):
                for n in parts:
                    if n >= 2:
                        act.wait_ge(h1_lo_ready, u * N1 + n - 1)
                    act.wait_ge(layer1_done, u * N1 + n + 1)
                    out = layer[:, n % 2, 0:UNIT]
                    nc.scalar.activation(h1_f[:, n % 2, :], out, ACT.Relu, bias=b1_sb[:, n:n + 1])\
                      .then_inc(h1_f_ready, 1)
                    nc.scalar.activation(h1_hi[:, n, :], out, ACT.Relu, bias=b1_sb[:, n:n + 1])\
                      .then_inc(h1_hi_ready, 1)

            def h2_out(u):
                act.wait_ge(y_free, u + 1)
                for m in range(N2):
                    act.wait_ge(layer2_done, u * N2 + m + 1)
                    nc.scalar.activation(h2_sb[:, m, :], layer[:, m % 2, 0:UNIT], ACT.Relu,
                                         bias=b2_sb[:, m:m + 1]).then_inc(h2_ready, 1)

            def y_row(u):
                act.wait_ge(layer3_done, u + 1)
                nc.scalar.activation(y_sb, layer[0:1, 0, 0:UNIT], ACT.Copy).then_inc(y_ready, 1)

            def next_item(u, n):
                if n == 0:
                    act.wait_ge(gram_ready, (u + 1) * BANKS)
                if n == 1:
                    act.wait_ge(bot_lo_ready, u + 1)
                to_xt(u + 1, n, ITEMS[n])

            def step(u, par):
                for n, item in enumerate(EARLY if last_unit(u) else ITEMS):
                    if n < AHEAD:
                        continue
                    if item == LOOKS[-1]:
                        if not last_unit(u):
                            next_ids(u)
                        if not (first(u) or last_unit(u)):
                            pairs_high(u - 1)
                    to_xt(u, n, item)
                if last_unit(u):
                    for n in (0, 1):
                        to_xt(u, len(EARLY) + n, TURN1[n])
                    act.wait_ge(packed[0], u * len(PACKS[0]) * 16)
                    gram_copies(u, (0,))
                    pairs_high(u - 1)
                    gram_copies(u, (2,))
                    for n in range(2, TURNS):
                        to_xt(u, len(EARLY) + n, TURN1[n])
                    h1_high(u - 1, (0,))
                    gram_copies(u, (4, 6))
                    h1_high(u - 1, (1, 2, 3))
                    bottom_high(u)
                    h2_out(u - 1)
                    return
                if first(u):
                    w1_high()
                else:
                    h1_high(u - 1, (0,))
                gram_copies(u, (0, 2))
                if not first(u):
                    h1_high(u - 1, (1, 2))
                next_item(u, 0)
                if not first(u):
                    h1_high(u - 1, (3,))
                bottom_high(u)
                next_item(u, 1)
                next_item(u, 2)
                if not first(u):
                    h2_out(u - 1)
                next_item(u, 3)
                next_item(u, 4)
                if not first(u):
                    y_row(u - 1)

            act.wait_ge(tab_split, K)
            for n in range(AHEAD):
                to_xt(0, n, ITEMS[n])
            over_units(act, step)
            pairs_high(UNITS - 1)
            y_row(UNITS - 2)
            h1_high(UNITS - 1, range(N1))
            h2_out(UNITS - 1)
            y_row(UNITS - 1)

        @block.vector
        def _(dve):
            nc.vector.memset(w1_stage, 0.0).then_inc(stage_zero, 1)
            nc.vector.memset(pairs[:, :, :, :].rearrange("p q c x -> p (q c x)"), 0.0).then_inc(pad_zero, 1)
            nc.vector.memset(grams[:, 0, :], 0.0).then_inc(pad_zero, 1)
            nc.vector.memset(grams[:, 1, :], 0.0).then_inc(pad_zero, 1)
            dve.wait_ge(rows_made, 1)
            nc.vector.tensor_copy(row_of[:, 0:RCH], row_i[:, :]).then_inc(rows_ready, 1)
            dve.wait_ge(rows_ready, 1)

            def one_hot(u, n):
                t, c = n * HOT // RCH, n * HOT % RCH
                before, unit = (n - RING, u) if n >= RING else (n - RING + PIECES, u - 1)
                if n == 0:
                    dve.wait_ge(ids_in, (u + 1) * 16)
                if not first(u) or before == n - RING:
                    used = looked_up if before % 2 else hot_first_used
                    dve.wait_ge(used, unit * K + before // 2 + 1)
                nc.vector.tensor_tensor(
                    hot[:, n % RING, :, :],
                    id_bc[0:RP, t, :].unsqueeze(1).broadcast_to([RP, HOT, UNIT]),
                    row_of[0:RP, c:c + HOT].unsqueeze(2).broadcast_to([RP, HOT, UNIT]),
                    ALU.is_equal).then_inc(hot_ready, 1)

            for n in range(RING):
                one_hot(0, n)
            for t in range(K):
                dve.wait_ge(tab_hi_done, t + 1)
                nc.vector.tensor_tensor(tab_lo[:, t, :], tab_stage[t], tab_hi[:, t, :].bitcast(f32),
                                        ALU.subtract).then_inc(tab_split, 1)
                if t < 4:
                    one_hot(0, RING + t)
            dve.wait_ge(w_hi_done, 1)
            nc.vector.tensor_tensor(
                w2_lo[:, :, :].rearrange("p k n -> p (k n)"), w2_stage,
                w2_hi[:, :, :].rearrange("p k n -> p (k n)").bitcast(f32), ALU.subtract).then_inc(w_split, 1)
            for n in range(RING + 4, PIECES):
                one_hot(0, n)

            def w1_low():
                dve.wait_ge(w_hi_done, 3)
                nc.vector.tensor_tensor(
                    w1_lo[:, 0:PACK, :].rearrange("p c n -> p (c n)"), w1_stage,
                    w1_hi[:, 0:PACK, :].rearrange("p c n -> p (c n)").bitcast(f32), ALU.subtract)
                nc.vector.tensor_tensor(w1_lo[:, PACK, :], bottom_stage, w1_hi[:, PACK, :].bitcast(f32),
                                        ALU.subtract).then_inc(w_split, 1)

            def gram_copies(u, fills):
                for n in fills:
                    copy_gram(dve, nc.vector.tensor_copy, u, n)

            def pairs_low(u):
                all_packed(dve, u)
                for c in range(PACK):
                    dve.wait_ge(pairs_hi_ready, u * PACK + c + 1)
                    nc.vector.tensor_tensor(
                        pairs_lo[:, c, :].rearrange("p (q x) -> p q x", q=Q), pairs[:, :, c, :],
                        pairs_hi[:, c, :].rearrange("p (q x) -> p q x", q=Q).bitcast(f32),
                        ALU.subtract).then_inc(pairs_lo_ready, 1)

            def bottom_low(u):
                dve.wait_ge(bot_hi_ready, u + 1)
                nc.vector.tensor_tensor(bot_lo[:, :], xt[:, :, 0], bot_hi[:, :].bitcast(f32),
                                        ALU.subtract).then_inc(bot_lo_ready, 1)

            def h1_low(u, parts):
                for n in parts:
                    dve.wait_ge(h1_f_ready, u * N1 + n + 1)
                    dve.wait_ge(h1_hi_ready, u * N1 + n + 1)
                    nc.vector.tensor_tensor(h1_lo[:, n, :], h1_f[:, n % 2, :], h1_hi[:, n, :].bitcast(f32),
                                            ALU.subtract).then_inc(h1_lo_ready, 1)

            def one_hots(u, pieces):
                for n in pieces:
                    one_hot(u, n)

            def step(u, par):
                if first(u):
                    w1_low()
                else:
                    one_hots(u, range(6, PIECES))
                    if last_unit(u):
                        dve.wait_ge(packed[0], u * len(PACKS[0]) * 16)
                        gram_copies(u, (1,))
                    pairs_low(u - 1)
                if last_unit(u):
                    gram_copies(u, (3,))
                    h1_low(u - 1, (0,))
                    gram_copies(u, (5, 7))
                    h1_low(u - 1, (1, 2, 3))
                    bottom_low(u)
                    return
                if not first(u):
                    h1_low(u - 1, (0,))
                gram_copies(u, (1, 3))
                one_hots(u + 1, (0, 1))
                if not first(u):
                    h1_low(u - 1, (1, 2))
                one_hots(u + 1, (2, 3))
                if not first(u):
                    h1_low(u - 1, (3,))
                bottom_low(u)
                one_hots(u + 1, (4, 5))

            over_units(dve, step)
            pairs_low(UNITS - 1)
            h1_low(UNITS - 1, range(N1))

        @block.tensor
        def _(pe):
            pe.wait_ge(ident_ready, 1)
            pe.wait_ge(pad_zero, 3)

            def turn(u, par, n, h, g):
                s = par * HALVES + h
                if g == 0:
                    pe.wait_ge(bottom_in[s], (u - par) * 8 + 16)
                e = places_of(g)
                pe.wait_ge(gathered[s][g], ((u - par) * 8 + 16) * len([x for x in e if x]))
                for k, place in enumerate(e):
                    last = nc.tensor.transpose(turned[:, n % TURNED, k * P:(k + 1) * P],
                                               emb[s][:, place, :], ident[:, :])
                last.then_inc(turned_ready, 1)

            def look_up(u, n, t):
                out = turned[:, n % TURNED, 0:UNIT]
                if first(u):
                    pe.wait_ge(tab_split, t + 1)
                for c in range(RCH):
                    piece = (t * RCH + c) // HOT
                    if c % HOT == 0:
                        pe.wait_ge(hot_ready, u * PIECES + piece + 1)
                    for tab in (tab_hi, tab_lo):
                        last = nc.tensor.matmul(
                            out, tab[:, t, c * D:(c + 1) * D],
                            hot[:, piece % RING, c % HOT, :],
                            start=(c == 0 and tab is tab_hi), stop=(c == RCH - 1 and tab is tab_lo))
                    if c % HOT == HOT - 1 and c < RCH - 1:
                        last.then_inc(hot_first_used, 1)
                last.then_inc(looked_up, 1)

            def three_passes(out, terms, start=True, stop=True):
                passes = [(w, x) for whi, wlo, xhi, xlo in terms for w, x in ((whi, xhi), (wlo, xhi), (whi, xlo))]
                for n, (w, x) in enumerate(passes):
                    last = nc.tensor.matmul(out, w, x, start=(start and n == 0),
                                            stop=(stop and n == len(passes) - 1))
                return last

            def layer1(u, parts):
                for n in parts:
                    out, cols = layer[:, n % 2, 0:UNIT], slice(n * P, (n + 1) * P)
                    if n == 0:
                        if first(u):
                            pe.wait_ge(w_split, 2)
                        pe.wait_ge(bot_lo_ready, u + 1)
                    if n >= 2:
                        pe.wait_ge(h1_hi_ready, u * N1 + n - 1)
                    three_passes(out, [(w1_hi[:, PACK, cols], w1_lo[:, PACK, cols], bot_hi[:, :], bot_lo[:, :])],
                                 stop=False)
                    for c in range(PACK):
                        if n == 0:
                            pe.wait_ge(pairs_lo_ready, u * PACK + c + 1)
                        last = three_passes(
                            out, [(w1_hi[:, c, cols], w1_lo[:, c, cols], pairs_hi[:, c, :], pairs_lo[:, c, :])],
                            start=False, stop=(c == PACK - 1))
                    last.then_inc(layer1_done, 1)

            def layer2(u):
                pe.wait_ge(h1_hi_ready, u * N1 + N1 - 1)
                for m in range(N2):
                    cols = slice(m * P, (m + 1) * P)
                    for k in range(N1):
                        if m == 0:
                            pe.wait_ge(h1_lo_ready, u * N1 + k + 1)
                        last = three_passes(
                            layer[:, m % 2, 0:UNIT],
                            [(w2_hi[:, k, cols], w2_lo[:, k, cols], h1_hi[:, k, :], h1_lo[:, k, :])],
                            start=(k == 0), stop=(k == N1 - 1))
                    last.then_inc(layer2_done, 1)

            def layer3(u):
                for m in range(N2):
                    pe.wait_ge(h2_ready, u * N2 + m + 1)
                    last = nc.tensor.matmul(layer[0:1, 0, 0:UNIT], w3_sb[:, m:m + 1], h2_sb[:, m, :],
                                            start=(m == 0), stop=(m == N2 - 1))
                last.then_inc(layer3_done, 1)

            def gram(u, fills):
                for n in fills:
                    if not first(u) or n >= 2:
                        pe.wait_ge(gram_out[n % 2], u * (BANKS // 2) + n // 2)
                    tiles, at = fills_of(u)[n]
                    for x in range(XB):
                        for q in tiles:
                            b = q * QX + at + x
                            last = nc.tensor.matmul(
                                grams[QP * q:QP * q + J, n % 2, x * J:(x + 1) * J],
                                xt[:, b, 0:J], xt[:, b, 1:PLACES], start=True, stop=True)
                    last.then_inc(gram_ready, 1)

            def to_xt(u, par, n, item):
                kind, h, k = item
                if not first(u) or n >= TURNED:
                    pe.wait_ge(xt_ready, u * EVAC + n - TURNED + 1)
                if kind == "turn":
                    turn(u, par, n, h, k)
                else:
                    look_up(u, n, k)

            def step(u, par):
                for n, item in enumerate(EARLY if last_unit(u) else ITEMS):
                    if n >= AHEAD:
                        to_xt(u, par, n, item)
                if last_unit(u):
                    for n in (0, 1):
                        to_xt(u, par, len(EARLY) + n, TURN1[n])
                    pe.wait_ge(xt_ready, u * EVAC + len(EARLY))
                    gram(u, range(BANKS))
                    for n in range(2, TURNS):
                        to_xt(u, par, len(EARLY) + n, TURN1[n])
                    layer1(u - 1, (0,))
                    pe.wait_ge(xt_ready, (u + 1) * EVAC)
                    gram(u, range(BANKS, 2 * BANKS))
                    layer1(u - 1, (1, 2, 3))
                    layer2(u - 1)
                    layer3(u - 1)
                    return
                if not first(u):
                    layer1(u - 1, (0,))
                pe.wait_ge(xt_ready, (u + 1) * EVAC)
                gram(u, range(BANKS))
                if first(u):
                    pe.wait_ge(small_in, 3 * 16)
                    for n in range(AHEAD):
                        to_xt(u + 1, 1 - par, n, ITEMS[n])
                    return
                layer1(u - 1, (1, 2))
                to_xt(u + 1, 1 - par, 0, ITEMS[0])
                layer1(u - 1, (3,))
                to_xt(u + 1, 1 - par, 1, ITEMS[1])
                to_xt(u + 1, 1 - par, 2, ITEMS[2])
                layer2(u - 1)
                to_xt(u + 1, 1 - par, 3, ITEMS[3])
                to_xt(u + 1, 1 - par, 4, ITEMS[4])
                layer3(u - 1)

            for n in range(AHEAD):
                to_xt(0, 0, n, ITEMS[n])
            over_units(pe, step)
            pe.wait_ge(y_ready, UNITS - 1)
            layer1(UNITS - 1, range(N1))
            layer2(UNITS - 1)
            layer3(UNITS - 1)


TABLES = 26


def kernel(**inputs):
    import numpy as np
    import concourse.bacc as bacc
    from concourse.bass_utils import run_bass_kernel_spmd

    nc = bacc.Bacc("TRN2", target_bir_lowering=False, num_devices=1)
    arrays = {}

    def give(name, a):
        a = np.ascontiguousarray(a)
        arrays[name] = a
        return nc.dram_tensor(name, a.shape, mybir.dt.from_np(a.dtype), kind="ExternalInput").ap()

    def columns(a):
        return np.asarray(a).reshape(-1, 128).T

    large, small = choose_tables([inputs[f"tbl_{t}"].shape[0] for t in range(TABLES)])
    features = [0] + [t + 1 for t in large + small]
    places = len(features)
    order = pair_order(places, features)

    ids, w1 = np.asarray(inputs["ids"]), np.asarray(inputs["W_top1"])
    bottom = give("bottom", inputs["r_bottom_output"])
    y = nc.dram_tensor("y", (bottom.shape[0], 1), mybir.dt.float32, kind="ExternalOutput").ap()
    dlrm_tower(
        nc, bottom,
        give("ids_large", ids[:, large]),
        give("ids_small", ids[:, small].T),
        [give(f"tbl_{t}", inputs[f"tbl_{t}"]) for t in large],
        [give(f"tbl_{t}", inputs[f"tbl_{t}"]) for t in small],
        give("w1_pairs", w1[order]),
        give("w1_bottom", w1[len(order):]),
        give("b_top1", columns(inputs["b_top1"])),
        give("w_top2", inputs["W_top2"]),
        give("b_top2", columns(inputs["b_top2"])),
        give("w_top3", columns(inputs["W_top3"])),
        y)
    r = run_bass_kernel_spmd(nc, [arrays], core_ids=[0])
    return r.results[0]["y"]
```
